# Optimizing a Trainium2 kernel written in Bass

```python
import numpy as np
import jax
import jax.numpy as jnp

def _softmax(x, axis=-1):
    return jax.nn.softmax(x, axis=axis)

def _gelu(x):
    return jax.nn.gelu(x, approximate=True)

def _silu(x):
    return jax.nn.silu(x)

def _sigmoid(x):
    return jax.nn.sigmoid(x)

def _layernorm(x, axis=-1, eps=1e-05):
    m = jnp.mean(x, axis=axis, keepdims=True)
    v = jnp.var(x, axis=axis, keepdims=True)
    return (x - m) / jnp.sqrt(v + eps)

def _scatter_add(tgt, idx, src, axis=0):
    return tgt.at[idx].add(src)

def _segment_sum(src, seg, n):
    return jax.ops.segment_sum(src, seg, n)
kernel_name = 'mk_decoder_postln_d1_seqx_r4_1e8efe'

def setup_inputs(seed: int=0):
    np.random.seed(seed)
    _w = jnp.asarray

    def _rec_inputs():
        import jax
        import jax.numpy as jnp
        _rk = jax.random.key(seed)
        x = 7.22e-05 + 1 * jax.random.normal(jax.random.fold_in(_rk, 1), (16, 112, 1024), jnp.float32)
        _lenS = 112 - jax.random.randint(jax.random.fold_in(_rk, 7), (16,), 0, max(1, 112 // 4) + 1, jnp.int32)
        _lenS2 = 375 - jax.random.randint(jax.random.fold_in(_rk, 8), (16,), 0, max(1, 375 // 4) + 1, jnp.int32)
        _ctx_4096P = jax.random.normal(jax.random.fold_in(_rk, 11), (16, 16, 1024), jnp.float32)
        _ctx_4096c = jax.random.dirichlet(jax.random.fold_in(_rk, 511), 0.3 * jnp.ones((16,), jnp.float32), (16, 375))
        _ctx_4096t = jnp.einsum('bsk,bkd->bsd', _ctx_4096c, _ctx_4096P)
        _ctx_4096t = _ctx_4096t * jax.lax.rsqrt(jnp.mean(jnp.square(_ctx_4096t)) + 1e-12) * 0.953939
        ctx_4096 = 4.13588e-05 + 0.999923 * (_ctx_4096t + 0.3 * jax.random.normal(jax.random.fold_in(_rk, 611), (16, 375, 1024), jnp.float32))
        return (x, ctx_4096)
    x, ctx_4096 = _rec_inputs()

    def _L0_attn_setup():
        import jax, jax.numpy as jnp
        import numpy as np
        K_FACTOR = 0.5
        key = jax.random.key(seed)
        k1, k2, k3, k4 = jax.random.split(key, 4)
        B, S, H, I = (1, 512, 1024, 2752)
        x = jax.random.normal(k1, (B, S, H), dtype=jnp.float32)
        w_gate = jax.random.normal(k2, (I, H), dtype=jnp.float32) * 0.02
        w_up = jax.random.normal(k3, (I, H), dtype=jnp.float32) * 0.02
        w_down = jax.random.normal(k4, (H, I), dtype=jnp.float32) * 0.02
        return {'x': x, 'w_gate': w_gate, 'w_up': w_up, 'w_down': w_down}
    _L0_attn_all = _L0_attn_setup()
    _L0_attn_in = {k: v for k, v in _L0_attn_all.items() if k in ('w_gate', 'w_up', 'w_down')}
    del _L0_attn_all

    def _L0_xattn_setup():
        import jax, jax.numpy as jnp
        import numpy as np
        DIM = 1024
        NUM_HEADS = 32
        NUM_KV_HEADS = 8
        HEAD_DIM = DIM // NUM_HEADS
        KV_DIM = DIM // (NUM_HEADS // NUM_KV_HEADS)
        B, S = (1, 512)
        key = jax.random.key(seed)
        ks = jax.random.split(key, 7)
        w_scale = DIM ** (-0.5)
        return {'query': jax.random.normal(ks[0], (B, S, DIM), jnp.float32), 'key': jax.random.normal(ks[1], (B, S, DIM), jnp.float32), 'value': jax.random.normal(ks[2], (B, S, DIM), jnp.float32), 'Wq': jax.random.normal(ks[3], (DIM, DIM), jnp.float32) * w_scale, 'Wk': jax.random.normal(ks[4], (DIM, KV_DIM), jnp.float32) * w_scale, 'Wv': jax.random.normal(ks[5], (DIM, KV_DIM), jnp.float32) * w_scale, 'Wo': jax.random.normal(ks[6], (DIM, DIM), jnp.float32) * w_scale}
    _L0_xattn_all = _L0_xattn_setup()
    _L0_xattn_in = {k: v for k, v in _L0_xattn_all.items() if k in ('Wq', 'Wk', 'Wv', 'Wo')}
    del _L0_xattn_all

    def _L0_ffn_setup():
        import jax, jax.numpy as jnp
        import numpy as np
        IN_FEATURES = 1024
        OUT_FEATURES = 1024
        GROUP_SIZE = 128
        PACKED_COLS = IN_FEATURES // 8
        GROUP_COUNT = IN_FEATURES // GROUP_SIZE

        def _dequantize(qweight, qscale, qzeros):
            out_f, packed_cols = qweight.shape
            in_f = packed_cols * 8
            shifts = jnp.arange(0, 32, 4, dtype=jnp.int32)
            w_int = (qweight[:, :, None] >> shifts & 15).reshape(out_f, in_f).astype(jnp.float32)
            w_int = w_int[:, :IN_FEATURES]
            gids = jnp.arange(IN_FEATURES, dtype=jnp.int32) // GROUP_SIZE
            scales = qscale[gids].T
            zeros = qzeros[gids].astype(jnp.float32).T
            return (w_int - zeros) * scales
        key = jax.random.key(seed)
        k1, k2, k3, k4 = jax.random.split(key, 4)
        x = jax.random.normal(k1, (4, 512, IN_FEATURES), dtype=jnp.float32)
        qweight = jax.random.randint(k2, (OUT_FEATURES, PACKED_COLS), jnp.iinfo(jnp.int32).min, jnp.iinfo(jnp.int32).max, dtype=jnp.int32)
        qscale = (jax.random.uniform(k3, (GROUP_COUNT, OUT_FEATURES), dtype=jnp.float32) + 0.5) * 0.01
        qzeros = jax.random.randint(k4, (GROUP_COUNT, OUT_FEATURES), 0, 16, dtype=jnp.int32)
        return {'x': x, 'qweight': qweight, 'qscale': qscale, 'qzeros': qzeros}
    _L0_ffn_all = _L0_ffn_setup()
    _L0_ffn_in = {k: v for k, v in _L0_ffn_all.items() if k in ('qweight', 'qscale', 'qzeros')}
    del _L0_ffn_all
    return {'x': x, 'ctx_4096': ctx_4096, 'L0_attn_w_gate': _L0_attn_in['w_gate'], 'L0_attn_w_up': _L0_attn_in['w_up'], 'L0_attn_w_down': _L0_attn_in['w_down'], 'L0_xattn_Wq': _L0_xattn_in['Wq'], 'L0_xattn_Wk': _L0_xattn_in['Wk'], 'L0_xattn_Wv': _L0_xattn_in['Wv'], 'L0_xattn_Wo': _L0_xattn_in['Wo'], 'L0_ffn_qweight': _L0_ffn_in['qweight'], 'L0_ffn_qscale': _L0_ffn_in['qscale'], 'L0_ffn_qzeros': _L0_ffn_in['qzeros']}

def reference(x, ctx_4096, L0_attn_w_gate, L0_attn_w_up, L0_attn_w_down, L0_xattn_Wq, L0_xattn_Wk, L0_xattn_Wv, L0_xattn_Wo, L0_ffn_qweight, L0_ffn_qscale, L0_ffn_qzeros):
    import jax
    import jax.numpy as jnp

    def _L0_attn_ref(x, w_gate, w_up, w_down):
        import jax, jax.numpy as jnp
        import numpy as np
        K_FACTOR = 0.5
        s = jax.nn.silu(jnp.einsum('bsh,ih->bsi', x, w_gate))
        B, S, I = s.shape
        k = int(K_FACTOR * I)
        _, idx = jax.lax.top_k(-jnp.abs(s), k)
        flat = s.reshape(B * S, I)
        rows = jnp.arange(B * S)[:, None]
        flat = flat.at[rows, idx.reshape(B * S, k)].set(0.0)
        s = flat.reshape(B, S, I)
        s = s * jnp.einsum('bsh,ih->bsi', x, w_up)
        return jnp.einsum('bsi,hi->bsh', s, w_down)

    def _L0_xattn_ref(query, key, value, Wq, Wk, Wv, Wo):
        import jax, jax.numpy as jnp
        import numpy as np
        DIM = 1024
        NUM_HEADS = 32
        NUM_KV_HEADS = 8
        HEAD_DIM = DIM // NUM_HEADS
        KV_DIM = DIM // (NUM_HEADS // NUM_KV_HEADS)
        B, S = (1, 512)
        b, sq, _ = query.shape
        _, sk, _ = key.shape
        rep = NUM_HEADS // NUM_KV_HEADS
        q = (query @ Wq).reshape(b, sq, NUM_HEADS, HEAD_DIM).transpose(0, 2, 1, 3)
        k = (key @ Wk).reshape(b, sk, NUM_KV_HEADS, HEAD_DIM).transpose(0, 2, 1, 3)
        v = (value @ Wv).reshape(b, sk, NUM_KV_HEADS, HEAD_DIM).transpose(0, 2, 1, 3)
        k = jnp.repeat(k, rep, axis=1)
        v = jnp.repeat(v, rep, axis=1)
        scale = HEAD_DIM ** (-0.5)
        scores = jnp.einsum('bhqd,bhkd->bhqk', q, k) * scale
        probs = jax.nn.softmax(scores, axis=-1)
        out = jnp.einsum('bhqk,bhkd->bhqd', probs, v)
        out = out.transpose(0, 2, 1, 3).reshape(b, sq, DIM)
        return out @ Wo

    def _L0_ffn_ref(x, qweight, qscale, qzeros):
        import jax, jax.numpy as jnp
        import numpy as np
        IN_FEATURES = 1024
        OUT_FEATURES = 1024
        GROUP_SIZE = 128
        PACKED_COLS = IN_FEATURES // 8
        GROUP_COUNT = IN_FEATURES // GROUP_SIZE

        def _dequantize(qweight, qscale, qzeros):
            out_f, packed_cols = qweight.shape
            in_f = packed_cols * 8
            shifts = jnp.arange(0, 32, 4, dtype=jnp.int32)
            w_int = (qweight[:, :, None] >> shifts & 15).reshape(out_f, in_f).astype(jnp.float32)
            w_int = w_int[:, :IN_FEATURES]
            gids = jnp.arange(IN_FEATURES, dtype=jnp.int32) // GROUP_SIZE
            scales = qscale[gids].T
            zeros = qzeros[gids].astype(jnp.float32).T
            return (w_int - zeros) * scales
        w = _dequantize(qweight, qscale, qzeros).astype(jnp.bfloat16)
        y = jnp.einsum('bsi,oi->bso', x.astype(jnp.bfloat16), w)
        return y.astype(x.dtype)
    x = _layernorm(x + _L0_attn_ref(x, L0_attn_w_gate, L0_attn_w_up, L0_attn_w_down), axis=-1)
    x = _layernorm(x + _L0_xattn_ref(x, ctx_4096, ctx_4096, L0_xattn_Wq, L0_xattn_Wk, L0_xattn_Wv, L0_xattn_Wo), axis=-1)
    x = _layernorm(x + _L0_ffn_ref(x, L0_ffn_qweight, L0_ffn_qscale, L0_ffn_qzeros), axis=-1)
    return x

_drawn_inputs = setup_inputs


def setup_inputs(seed=0):
    import zlib

    import numpy as np

    out = dict(_drawn_inputs(seed))
    spreads = {}
    factors = {}
    for name, (base, spread) in spreads.items():
        noise = np.random.default_rng([zlib.crc32(name.encode()), seed]).standard_normal(out[name].shape)
        drawn = base * np.exp(spread * noise) if base else spread * noise
        out[name] = jnp.asarray(drawn.astype(out[name].dtype))
    for name, factor in factors.items():
        out[name] = (out[name] * factor).astype(out[name].dtype)
    return out
```

```python
from contextlib import ExitStack

import concourse.bass as bass
from concourse import mybir

F32 = mybir.dt.float32
F32R = mybir.dt.float32r
BF16 = mybir.dt.bfloat16
I32 = mybir.dt.int32
I16 = mybir.dt.int16
ALU = mybir.AluOpType
ACT = mybir.ActivationFunctionType
AX_X = mybir.AxisListType.X

P = 128
B, S, D = 16, 112, 1024
C = 375
CP = C + 1
I = 2752
KD = D // P
MI = (I + P - 1) // P
MI_FULL = I // P
TAIL = I - MI_FULL * P
ZEROED = I // 2
G, GB = 4, 4
T = GB * S
H, KV, HD = 32, 8, 32
REP = H // KV
KT = 3
KN = C // KT
VW = 3 * HD
SCALE = float(HD) ** -0.5
EPS = 1e-5
QG = 128
NQ = D // QG


class Bufs:

    def __init__(self, nc, ctx, tag):
        self.nc, self.ctx, self.tag = nc, ctx, tag

    def sb(self, name, shape, dt):
        return self.ctx.enter_context(self.nc.sbuf_tensor(f"{self.tag}_{name}", shape, dt))

    def ps(self, name, shape, dt):
        return self.ctx.enter_context(self.nc.psum_tensor(f"{self.tag}_{name}", shape, dt))

    def sem(self, name):
        return self.ctx.enter_context(self.nc.semaphore(f"{self.tag}_{name}"))


def matmul3(nc, out, wh, wl, xh, xl, first, last):
    nc.tensor.matmul(out, wh, xh, start=first, stop=False)
    nc.tensor.matmul(out, wh, xl, start=False, stop=False)
    return nc.tensor.matmul(out, wl, xh, start=False, stop=last)


def dequant_pass(nc, q_weight, q_scale, q_zero, ident_b, w3_dram):
    with ExitStack() as ctx:
        m = Bufs(nc, ctx, "dq")
        packed = m.sb("packed", [P, KD, P], I32)
        nib = m.sb("nib", [P, KD, D], I32)
        scale = m.sb("scale", [P, KD, NQ], F32)
        zero_i = m.sb("zero_i", [P, KD, NQ], I32)
        zero = m.sb("zero", [P, KD, NQ], F32)
        w_oi = m.sb("w_oi", [P, KD, D], BF16)
        w_io = m.sb("w_io", [P, KD, D], BF16)
        pt = [m.ps(f"pt{i}", [P, KD, P], BF16) for i in range(2)]
        loaded, unpacked, tr, copied, stored = (m.sem(n) for n in ("loaded", "unpacked", "tr", "copied", "stored"))
        block = ctx.enter_context(nc.Block())

        @block.sync
        def _(sp):
            sp.dma_start(packed[:], q_weight.rearrange("(o p) c -> p o c", p=P)).then_inc(loaded, 16)
            sp.dma_start(scale[:], q_scale).then_inc(loaded, 16)
            sp.dma_start(zero_i[:], q_zero).then_inc(loaded, 16)
            sp.wait_ge(copied, KD)
            sp.dma_start(w3_dram, w_io[:]).then_inc(stored, 16)
            sp.wait_ge(stored, 16)

        @block.vector
        def _(dve):
            dve.wait_ge(loaded, 48)
            nib_v = nib[:].rearrange("p o (c s) -> p o c s", s=8)
            for s in range(8):
                nc.vector.tensor_scalar(nib_v[:, :, :, s], packed[:], 4 * s, 15,
                                        ALU.logical_shift_right, ALU.bitwise_and)
            nc.vector.tensor_copy(zero[:], zero_i[:])
            dve.drain()
            for o in range(KD):
                for q in range(NQ):
                    cols = slice(q * QG, (q + 1) * QG)
                    last = nc.vector.tensor_scalar(w_oi[:, o, cols], nib[:, o, cols], zero[:, o, q:q + 1],
                                                   scale[:, o, q:q + 1], ALU.subtract, ALU.mult)
                last.then_inc(unpacked, 1)

        @block.tensor
        def _(pe):
            for k in range(KD):
                if k == 0:
                    pe.wait_ge(unpacked, KD)
                if k >= 2:
                    pe.wait_ge(copied, k - 1)
                for o in range(KD):
                    last = nc.tensor.transpose(pt[k % 2][:, o, :], w_oi[:, o, k * P:(k + 1) * P], ident_b[:])
                last.then_inc(tr, 1)

        @block.scalar
        def _(act):
            for k in range(KD):
                act.wait_ge(tr, k + 1)
                nc.scalar.copy(w_io[:, k, :], pt[k % 2][:].rearrange("p o c -> p (o c)")).then_inc(copied, 1)


def context_pass(nc, ctx_t, w_kv, kd, vd):
    KVD = KV * HD
    NB = 5
    with ExitStack() as ctx:
        m = Bufs(nc, ctx, "cp")
        w_raw = m.sb("w_raw", [P, KD, 2 * KVD], F32)
        w_hi = m.sb("w_hi", [P, KD, 2 * KVD], F32R)
        w_lo = m.sb("w_lo", [P, KD, 2 * KVD], F32R)
        c_raw = [m.sb(f"c_raw{i}", [P, KD, CP], F32) for i in range(2)]
        c_hi = [m.sb(f"c_hi{i}", [P, KD, CP], F32R) for i in range(2)]
        c_lo = [m.sb(f"c_lo{i}", [P, KD, CP], F32R) for i in range(2)]
        k_out = [m.sb(f"k_out{i}", [P, 2, 2, CP], F32R) for i in range(2)]
        v_out = [m.sb(f"v_out{i}", [KN, KT, KV, VW], F32) for i in range(2)]
        pk = [m.ps(f"pk{i}", [P, 512], F32) for i in range(2)]
        pv = [m.ps(f"pv{i}", [P, 512], F32) for i in range(KT)]
        w_loaded, w_hi_done, w_split, pads = (m.sem(n) for n in ("w_loaded", "w_hi_done", "w_split", "pads"))
        loaded = [m.sem(f"loaded{i}") for i in range(2)]
        stored = [m.sem(f"stored{i}") for i in range(2)]
        hi_done, lo_done, used, proj, evac = (m.sem(n) for n in ("hi_done", "lo_done", "used", "proj", "evac"))
        block = ctx.enter_context(nc.Block())
        PAIRS = B // 2

        @block.sync
        def _(sp):
            def load(n, p):
                sp.wait_ge(lo_done, n + 1)
                sp.dma_start(c_raw[p][:, :, 0:C], ctx_t[n]).then_inc(loaded[p], 16)

            def store(n, p):
                sp.wait_ge(evac, NB * (n + 2))
                sp.dma_start(kd[n], k_out[p][:].bitcast(F32).rearrange("p m h c -> p (m h c)")).then_inc(stored[p], 16)
                sp.dma_start(vd[n], v_out[p][:].rearrange("p t v w -> p (t v w)")).then_inc(stored[p], 16)

            for s in stored:
                sp.sem_inc(s, 1)
            sp.dma_start(w_raw[:], w_kv).then_inc(w_loaded, 16)
            sp.wait_ge(pads, 4)
            load(0, 0)
            with sp.Fori(0, PAIRS - 1) as i:
                load(2 * i + 1, 1)
                store(2 * i, 0)
                load(2 * i + 2, 0)
                store(2 * i + 1, 1)
            load(B - 1, 1)
            store(B - 2, 0)
            store(B - 1, 1)
            sp.wait_ge(stored[0], 32 * PAIRS + 1)
            sp.wait_ge(stored[1], 32 * PAIRS + 1)

        @block.scalar
        def _(act):
            act.wait_ge(w_loaded, 16)
            nc.scalar.copy(w_hi[:], w_raw[:]).then_inc(w_hi_done, 1)

            with act.Fori(0, PAIRS) as i:
                for p in range(2):
                    act.wait_ge(loaded[p], 16 * i + 16)
                    act.wait_ge(used, 2 * i + p + 1)
                    nc.scalar.copy(c_hi[p][:], c_raw[p][:]).then_inc(hi_done, 1)

        @block.gpsimd
        def _(pool):
            pool.sem_inc(lo_done, 2)
            for p in range(2):
                nc.gpsimd.memset(c_raw[p][:, :, C:CP], 0.0).then_inc(pads, 1)
                nc.gpsimd.memset(v_out[p][:, :, :, HD:VW], 1.0).then_inc(pads, 1)
            pool.wait_ge(w_hi_done, 1)
            nc.gpsimd.tensor_tensor(w_lo[:], w_raw[:], w_hi[:].bitcast(F32), ALU.subtract).then_inc(w_split, 1)
            with pool.Fori(0, PAIRS) as i:
                for p in range(2):
                    pool.wait_ge(hi_done, 2 * i + p + 1)
                    nc.gpsimd.tensor_tensor(c_lo[p][:], c_raw[p][:], c_hi[p][:].bitcast(F32),
                                            ALU.subtract).then_inc(lo_done, 1)

        @block.tensor
        def _(pe):
            pe.sem_inc(used, 2)
            pe.wait_ge(w_split, 1)
            with pe.Fori(0, PAIRS) as i:
                for p in range(2):
                    pe.wait_ge(lo_done, 2 * i + p + 3)
                    for j in range(2):
                        pe.wait_ge(evac, NB * (2 * i + p) + j + 1)
                        for k in range(KD):
                            w = slice(j * P, (j + 1) * P)
                            last = matmul3(nc, pk[j][:, 0:CP], w_hi[:, k, w], w_lo[:, k, w],
                                           c_hi[p][:, k, :], c_lo[p][:, k, :], k == 0, k == KD - 1)
                        last.then_inc(proj, 1)
                    for t in range(KT):
                        pe.wait_ge(evac, NB * (2 * i + p) + 3 + t)
                        for k in range(KD):
                            c = slice(t * KN, (t + 1) * KN)
                            last = matmul3(nc, pv[t][0:KN, 0:KVD], c_hi[p][:, k, c], c_lo[p][:, k, c],
                                           w_hi[:, k, KVD:], w_lo[:, k, KVD:], k == 0, k == KD - 1)
                        last.then_inc(proj, 1)
                    pe.drain().then_inc(used, 1)

        @block.vector
        def _(dve):
            dve.sem_inc(evac, NB)
            dve.wait_ge(pads, 4)
            with dve.Fori(0, PAIRS) as i:
                for p in range(2):
                    dve.wait_ge(stored[p], 32 * i + 1)
                    for j in range(2):
                        dve.wait_ge(proj, NB * (2 * i + p) + j + 1)
                        nc.vector.tensor_copy(k_out[p][:, j, 0, :], pk[j][:, 0:CP])
                        dve.drain()
                        nc.vector.tensor_tensor(k_out[p][:, j, 1, :], pk[j][:, 0:CP],
                                                k_out[p][:, j, 0, :].bitcast(F32), ALU.subtract).then_inc(evac, 1)
                    for t in range(KT):
                        dve.wait_ge(proj, NB * (2 * i + p) + 3 + t)
                        nc.vector.tensor_copy(v_out[p][:, t, :, 0:HD],
                                              pv[t][0:KN, 0:KVD].rearrange("p (v d) -> p v d", d=HD)).then_inc(evac, 1)


class Selection:

    AIM = ZEROED + 3.5
    GAINS = (1.0, 1.0, 0.7, 0.5, 0.4, 0.25)
    MEDIAN = 0.7526
    DENSITY = 1903.0
    SAMPLE = 512

    def __init__(self, nc, dve, m, keys, keep, scratch):
        self.nc, self.dve, self.keys, self.keep, self.scratch = nc, dve, keys, keep, scratch
        f = lambda name, shape, dt=F32: m.sb("sel_" + name, shape, dt)
        self.found, self.bit, self.trial, self.low = (f(n, [S, GB], I32) for n in ("found", "bit", "trial", "low"))
        self.left, self.count, self.bound, self.unit, self.off, self.off2, self.key = (
            f(n, [S, GB]) for n in ("left", "count", "bound", "unit", "off", "off2", "key"))
        self.top = f("top", [S, GB, 8])
        self.order = f("order", [S, 8])
        self.pick = f("pick", [S, GB, 8])
        self.bad = f("bad", [P, 32])
        self.bad_turned = f("bad_turned", [P, 32])
        self.bad_any = f("bad_any", [P, 1], I32)

    def start(self):
        nc = self.nc
        nc.vector.memset(self.bad[:], 0.0)
        for n in range(8):
            nc.vector.memset(self.order[:, n:n + 1], float(n))
        self.dve.drain()

    def count_keys(self, bound, op):
        for b in range(GB):
            self.nc.vector.tensor_scalar(self.keep[:, b, 0:I], self.keys[:, b, :], bound[:, b:b + 1], None,
                                         op, ALU.add, accum_out=self.count[:, b:b + 1])
        self.dve.drain()

    def fast(self):
        nc, dve = self.nc, self.dve
        nc.vector.tensor_reduce(self.unit[:], self.keys[:, :, 0:self.SAMPLE], AX_X, ALU.add)
        dve.drain()
        nc.vector.tensor_scalar(self.bound[:], self.unit[:], self.MEDIAN / self.SAMPLE, None, ALU.mult)
        nc.vector.tensor_scalar(self.unit[:], self.unit[:], 1.0 / (self.SAMPLE * self.DENSITY), None, ALU.mult)
        dve.drain()
        for gain in self.GAINS:
            self.count_keys(self.bound[:], ALU.is_le)
            nc.vector.tensor_scalar(self.off[:], self.count[:], self.AIM, gain, ALU.subtract, ALU.mult)
            dve.drain()
            nc.vector.tensor_tensor(self.off2[:], self.off[:], self.off[:], ALU.mult)
            nc.vector.tensor_tensor(self.key[:], self.off[:], self.unit[:], ALU.mult)
            dve.drain()
            nc.vector.scalar_tensor_tensor(out=self.off[:], in0=self.off2[:], scalar=(3.6 * gain) ** 2,
                                           in1=self.key[:], op0=ALU.is_gt, op1=ALU.mult)
            dve.drain()
            nc.vector.tensor_tensor(self.bound[:], self.bound[:], self.off[:], ALU.subtract)
            dve.drain()
        self.count_keys(self.bound[:], ALU.is_le)
        nc.vector.tensor_scalar(self.off[:], self.count[:], float(ZEROED), None, ALU.subtract)
        for b in range(GB):
            nc.vector.scalar_tensor_tensor(out=self.scratch[:], in0=self.keys[:, b, :], scalar=self.bound[:, b:b + 1],
                                           in1=self.keys[:, b, :], op0=ALU.is_le, op1=ALU.mult)
            dve.drain()
            nc.vector.max(self.top[:, b, :], self.scratch[:])
            dve.drain()
            nc.vector.scalar_tensor_tensor(out=self.pick[:, b, :], in0=self.order[:], scalar=self.off[:, b:b + 1],
                                           in1=self.top[:, b, :], op0=ALU.is_equal, op1=ALU.mult,
                                           accum_out=self.key[:, b:b + 1])
        dve.drain()
        self.count_keys(self.key[:], ALU.is_gt)
        nc.vector.tensor_scalar(self.off[:], self.count[:], float(I - ZEROED), None, ALU.not_equal)
        dve.drain()
        nc.vector.reduce_max(self.bad[0:S, 0:1], self.off[:], AX_X)
        dve.drain()
        nc.vector.transpose(self.bad_turned[:], self.bad[:])
        dve.drain()
        nc.vector.reduce_max(self.bad_any[:], self.bad_turned[:], AX_X)
        dve.drain()

    def any_bad(self):
        return sum((self.dve.value_load(self.bad_any[q:q + 1, 0:1], min_val=0, max_val=1)
                    for q in range(32, P, 32)), self.dve.value_load(self.bad_any[0:1, 0:1], min_val=0, max_val=1))

    def exact(self):
        nc, dve = self.nc, self.dve
        found, bit, trial, low = self.found[:], self.bit[:], self.trial[:], self.low[:]
        nc.vector.memset(found, 0)
        nc.vector.memset(bit, 1 << 30)
        with dve.Fori(0, 31):
            dve.drain()
            nc.vector.tensor_tensor(trial, found, bit, ALU.bitwise_or)
            dve.drain()
            self.count_keys(trial.bitcast(F32), ALU.is_lt)
            nc.vector.tensor_scalar(low, self.count[:], ZEROED - 0.5, -1.0, ALU.is_lt, ALU.mult)
            dve.drain()
            nc.vector.tensor_tensor(trial, low, bit, ALU.bitwise_and)
            dve.drain()
            nc.vector.tensor_tensor(found, found, trial, ALU.bitwise_or)
            nc.vector.tensor_scalar(bit, bit, 1, None, ALU.logical_shift_right)
        dve.drain()
        found = found.bitcast(F32)
        self.count_keys(found, ALU.is_lt)
        nc.vector.tensor_scalar(self.left[:], self.count[:], -1.0, float(ZEROED), ALU.mult, ALU.add)
        dve.drain()
        run = self.scratch[:].bitcast(I16)[:, 0:I]
        for b in range(GB):
            row = self.keep[:, b, 0:I]
            nc.vector.tensor_scalar(row, self.keys[:, b, :], found[:, b:b + 1], None, ALU.is_equal)
            dve.drain()
            nc.vector.tensor_tensor_scan(run, row, row, 0.0, ALU.add, ALU.max)
            dve.drain()
            nc.vector.scalar_tensor_tensor(out=row, in0=run, scalar=self.left[:, b:b + 1], in1=row,
                                           op0=ALU.is_gt, op1=ALU.mult)
            dve.drain()
            nc.vector.scalar_tensor_tensor(out=row, in0=self.keys[:, b, :], scalar=found[:, b:b + 1], in1=row,
                                           op0=ALU.is_gt, op1=ALU.add)
        dve.drain()


def gated_pass(nc, x_t, w_gu, w_d, w_d_tail, ident_f, ident_b, y_dram):
    DC = 3
    N_CH = 2 * MI + KD * DC
    RAW, SPL = 4, 2
    N_EV = 2 * MI + KD
    SPLIT_AT = {KD + 2: 2 * MI + 2, 2 * KD + 2: 2 * MI + 3}
    with ExitStack() as ctx:
        m = Bufs(nc, ctx, "gp")
        x_raw = m.sb("x_raw", [P, KD, T], F32)
        x_hi = m.sb("x_hi", [P, KD, T], F32R)
        x_lo = m.sb("x_lo", [P, KD, T], F32R)
        raw = [m.sb(f"raw{i}", [P, KD, P], F32) for i in range(RAW)]
        w_hi = [m.sb(f"w_hi{i}", [P, KD, P], F32R) for i in range(SPL)]
        w_lo = [m.sb(f"w_lo{i}", [P, KD, P], F32R) for i in range(SPL)]
        up = [m.sb(f"up{i}", [P, T], F32) for i in range(2)]
        y = [m.sb(f"y{i}", [P, T], F32) for i in range(2)]
        h = [m.sb(f"h{i}", [P, T], F32) for i in range(2)]
        keep = m.sb("keep", [S, GB, MI * P], BF16)
        scratch = m.sb("scratch", [S, I], F32)
        place = Bufs(nc, ctx, "gp")
        sel = Selection(nc, nc.vector, place, None, keep, scratch)
        with nc.sbuf_tensor("gp_act", [P, MI, T], F32) as act_t, nc.sbuf_tensor("gp_keys", [S, GB, I], F32) as keys:
            pass
        with nc.sbuf_tensor("gp_h_hi", [P, MI, T], F32R) as h_hi, nc.sbuf_tensor("gp_h_lo", [P, MI, T], F32R) as h_lo:
            pass
        sel.keys = keys
        acc = [m.ps(f"acc{i}", [P, 512], F32) for i in range(2)]
        ptr = [m.ps(f"ptr{i}", [S, GB, P], F32) for i in range(2)]
        pmk = [m.ps(f"pmk{i}", [P, GB, S], BF16) for i in range(2)]
        names = ("x_loaded", "x_hi_done", "x_lo_done", "hi_done", "lo_done", "used", "evac", "turned", "keyed",
                 "up_mul", "pads", "kept", "masks", "masked", "h_hi_done", "h_lo_done")
        (x_loaded, x_hi_done, x_lo_done, hi_done, lo_done, used, evac, turned, keyed,
         up_mul, pads, kept, masks, masked, h_hi_done, h_lo_done) = (m.sem(n) for n in names)
        raw_loaded = [m.sem(f"raw_loaded{i}") for i in range(RAW)]
        y_stored = [m.sem(f"y_stored{i}") for i in range(2)]
        block = ctx.enter_context(nc.Block())

        def rows(t):
            return P if t < MI_FULL else TAIL

        def tiles(c):
            return range(KD * c, min(KD * c + KD, MI))

        sums, upto = [0] * RAW, []
        for c in range(N_CH):
            sums[c % RAW] += 32 if c >= 2 * MI and (c - 2 * MI) % DC == DC - 1 else 16
            upto.append(sums[c % RAW])

        @block.sync
        def _(sp):
            def load_x(g):
                sp.wait_ge(x_lo_done, KD * g + 1)
                sp.dma_start(x_raw[:], x_t[g]).then_inc(x_loaded, 16)

            def store_y(g, j):
                sp.wait_ge(evac, N_EV * g + 2 * MI + j + 3)
                sp.dma_start(y_dram[g, j], y[j % 2][:]).then_inc(y_stored[j % 2], 16)

            for s in y_stored:
                sp.sem_inc(s, 1)
            with sp.Fori(0, G) as g:
                load_x(g)
                for c in range(N_CH):
                    slot, sem = raw[c % RAW], raw_loaded[c % RAW]
                    sp.wait_ge(lo_done, N_CH * g + c + 1)
                    if c < 2 * MI:
                        n = rows(c % MI)
                        sp.dma_start(slot[:, :, 0:n], w_gu[c // MI, :, :, (c % MI) * P:(c % MI) * P + n]
                                     if n < P else w_gu[c // MI, :, :, (c % MI) * P:(c % MI + 1) * P]).then_inc(sem, 16)
                    else:
                        j, cc = divmod(c - 2 * MI, DC)
                        full = [t for t in tiles(cc) if t < MI_FULL]
                        sp.dma_start(slot[:, 0:len(full), :], w_d[j, :, full[0]:full[-1] + 1, :]).then_inc(sem, 16)
                        if cc == DC - 1:
                            sp.dma_start(slot[0:TAIL, len(full), :], w_d_tail[j]).then_inc(sem, 16)
                            if j >= 2:
                                store_y(g, j - 2)
                store_y(g, KD - 2)
                store_y(g, KD - 1)
            for s in y_stored:
                sp.wait_ge(s, 16 * G * KD // 2 + 1)

        def part(t, c):
            if c < 2 * MI:
                return [t[:, :, 0:rows(c % MI)]]
            cc = (c - 2 * MI) % DC
            if cc < DC - 1:
                return [t[:, :, :]]
            n = len(tiles(cc)) - 1
            return [t[:, 0:n, :], t[0:TAIL, n, :]]

        @block.scalar
        def _(act):
            act.sem_inc(evac, 2)
            act.sem_inc(keyed, 2)
            with act.Fori(0, G) as g:
                def split_hi(c):
                    act.wait_ge(raw_loaded[c % RAW], sums[c % RAW] * g + upto[c])
                    act.wait_ge(used, N_CH * g + c + 1)
                    for o, i in zip(part(w_hi[c % SPL], c), part(raw[c % RAW], c)):
                        last = nc.scalar.copy(o, i)
                    last.then_inc(hi_done, 1)

                def make_keys(t):
                    n = rows(t)
                    act.wait_ge(turned, MI * g + t + 1)
                    nc.scalar.activation(keys[:, :, t * P:t * P + n], ptr[t % 2][:, :, 0:n],
                                         ACT.Abs).then_inc(keyed, 1)

                act.wait_ge(x_loaded, 16 * g + 16)
                act.wait_ge(used, N_CH * g + 2)
                for k in range(KD):
                    nc.scalar.copy(x_hi[:, k, :], x_raw[:, k, :]).then_inc(x_hi_done, 1)
                split_hi(0)
                split_hi(1)
                for c in range(MI):
                    n = rows(c)
                    act.wait_ge(used, N_CH * g + c + 3)
                    nc.scalar.activation(act_t[0:n, c, :], acc[c % 2][0:n, 0:T], ACT.Silu).then_inc(evac, 1)
                    split_hi(c + 2)
                    if c >= 1:
                        make_keys(c - 1)
                make_keys(MI - 1)
                for c in range(MI, 2 * MI):
                    n = rows(c - MI)
                    act.wait_ge(used, N_CH * g + c + 3)
                    act.wait_ge(up_mul, MI * g + c - MI + 1)
                    nc.scalar.copy(up[c % 2][0:n, :], acc[c % 2][0:n, 0:T]).then_inc(evac, 1)
                    split_hi(c + 2)
                for t in range(MI):
                    n = rows(t)
                    act.wait_ge(masked, MI * g + t + 3)
                    nc.scalar.copy(h_hi[0:n, t, :], h[t % 2][0:n, :]).then_inc(h_hi_done, 1)
                    if t in SPLIT_AT:
                        split_hi(SPLIT_AT[t])
                for j in range(KD):
                    for cc in range(DC):
                        c = 2 * MI + DC * j + cc
                        act.wait_ge(used, N_CH * g + c + 3)
                        if 2 * MI + 4 <= c + 2 < N_CH:
                            split_hi(c + 2)
                    act.wait_ge(y_stored[j % 2], 16 * (KD // 2) * g + 16 * (j // 2) + 1)
                    nc.scalar.copy(y[j % 2][:], acc[j % 2][:, 0:T]).then_inc(evac, 1)

        @block.gpsimd
        def _(pool):
            pool.sem_inc(x_lo_done, 1)
            pool.sem_inc(lo_done, RAW)
            pool.sem_inc(up_mul, 2)
            pool.sem_inc(h_lo_done, 2)
            nc.gpsimd.memset(act_t[TAIL:P, MI - 1, :], 0.0).then_inc(pads, 1)
            pool.wait_ge(pads, 1)
            nc.gpsimd.memset(keep[:, :, I:], 0.0).then_inc(pads, 1)
            pool.wait_ge(pads, 2)
            with pool.Fori(0, G) as g:
                def split_lo(c):
                    pool.wait_ge(hi_done, N_CH * g + c + 1)
                    for o, i, hi in zip(part(w_lo[c % SPL], c), part(raw[c % RAW], c), part(w_hi[c % SPL], c)):
                        last = nc.gpsimd.tensor_tensor(o, i, hi.bitcast(F32), ALU.subtract)
                    last.then_inc(lo_done, 1)

                for k in range(KD):
                    pool.wait_ge(x_hi_done, KD * g + k + 1)
                    nc.gpsimd.tensor_tensor(x_lo[:, k, :], x_raw[:, k, :], x_hi[:, k, :].bitcast(F32),
                                            ALU.subtract).then_inc(x_lo_done, 1)
                split_lo(0)
                split_lo(1)
                for c in range(2 * MI):
                    split_lo(c + 2)
                    if c >= MI:
                        t, n = c - MI, rows(c - MI)
                        pool.wait_ge(evac, N_EV * g + c + 3)
                        nc.gpsimd.tensor_tensor(act_t[0:n, t, :], act_t[0:n, t, :], up[c % 2][0:n, :],
                                                ALU.mult).then_inc(up_mul, 1)
                for t in range(MI):
                    n = rows(t)
                    pool.wait_ge(h_hi_done, MI * g + t + 1)
                    nc.gpsimd.tensor_tensor(h_lo[0:n, t, :], h[t % 2][0:n, :], h_hi[0:n, t, :].bitcast(F32),
                                            ALU.subtract).then_inc(h_lo_done, 1)
                    if t in SPLIT_AT:
                        split_lo(SPLIT_AT[t])
                for c in range(2 * MI + 4, N_CH):
                    split_lo(c)

        @block.vector
        def _(dve):
            dve.sem_inc(masked, 2)
            sel.dve = dve
            sel.start()
            with dve.Fori(0, G) as g:
                dve.wait_ge(keyed, MI * g + MI + 2)
                sel.fast()
                with dve.If(sel.any_bad()):
                    sel.exact()
                dve.drain().then_inc(kept, 1)
                for t in range(MI):
                    n = rows(t)
                    dve.wait_ge(masks, MI * g + t + 1)
                    dve.wait_ge(up_mul, MI * g + t + 3)
                    dve.wait_ge(h_lo_done, MI * g + t + 1)
                    nc.vector.tensor_tensor(h[t % 2][0:n, :], act_t[0:n, t, :],
                                            pmk[t % 2][0:n].rearrange("p b s -> p (b s)"),
                                            ALU.mult).then_inc(masked, 1)

        @block.tensor
        def _(pe):
            pe.sem_inc(used, SPL)
            pe.wait_ge(pads, 2)
            with pe.Fori(0, G) as g:
                def turn(t):
                    pe.wait_ge(evac, N_EV * g + t + 3)
                    pe.wait_ge(keyed, MI * g + t + 1)
                    for b in range(GB):
                        last = nc.tensor.transpose(ptr[t % 2][:, b, :], act_t[:, t, b * S:(b + 1) * S], ident_f[:])
                    last.then_inc(turned, 1)

                def turn_mask(t):
                    pe.wait_ge(masked, MI * g + t + 1)
                    for b in range(GB):
                        last = nc.tensor.transpose(pmk[t % 2][:, b, :], keep[:, b, t * P:(t + 1) * P],
                                                   ident_b[0:S, 0:S])
                    last.then_inc(masks, 1)

                pe.wait_ge(x_lo_done, KD * g + KD + 1)
                for c in range(2 * MI):
                    n = rows(c % MI)
                    pe.wait_ge(lo_done, N_CH * g + c + RAW + 1)
                    pe.wait_ge(evac, N_EV * g + c + 1)
                    for k in range(KD):
                        last = matmul3(nc, acc[c % 2][0:n, 0:T], w_hi[c % SPL][:, k, 0:n], w_lo[c % SPL][:, k, 0:n],
                                       x_hi[:, k, :], x_lo[:, k, :], k == 0, k == KD - 1)
                    last.then_inc(used, 1)
                    if 1 <= c <= MI:
                        turn(c - 1)
                pe.wait_ge(kept, g + 1)
                turn_mask(0)
                turn_mask(1)
                for j in range(KD):
                    pe.wait_ge(evac, N_EV * g + 2 * MI + j + 1)
                    for cc in range(DC):
                        c = 2 * MI + DC * j + cc
                        pe.wait_ge(lo_done, N_CH * g + c + RAW + 1)
                        for t in tiles(cc):
                            n, s = rows(t), t - KD * cc
                            if j == 0:
                                if t + 2 < MI:
                                    turn_mask(t + 2)
                                pe.wait_ge(h_lo_done, MI * g + t + 3)
                            last = matmul3(nc, acc[j % 2][:, 0:T], w_hi[c % SPL][0:n, s, :], w_lo[c % SPL][0:n, s, :],
                                           h_hi[0:n, t, :], h_lo[0:n, t, :], t == 0, t == MI - 1)
                        last.then_inc(used, 1)


def layer_norm(nc, dve, src, stats, mv, var_eps, rstd, dst, ready, rooted, value):
    for n in range(2):
        nc.vector.bn_stats(stats[:, n, :], src[:, n * 512:(n + 1) * 512])
    dve.drain()
    nc.vector.bn_aggr(mv[:], stats[:].rearrange("p n s -> p (n s)"))
    dve.drain()
    nc.vector.tensor_scalar(var_eps[:], mv[:, 1:2], EPS, None, ALU.add).then_inc(ready, 1)
    dve.wait_ge(rooted, value)
    return nc.vector.tensor_scalar(dst, src, mv[:, 0:1], rstd[:, 0:1], ALU.subtract, ALU.mult)


def query_pass(nc, x_tok, y_dram, w_q, ident_f, y1_dram, qd):
    with ExitStack() as ctx:
        m = Bufs(nc, ctx, "qp")
        y_t = [m.sb(f"y_t{i}", [P, KD, T], F32) for i in range(1)]
        xs = m.sb("xs", [S, GB, D], F32)
        y1 = m.sb("y1", [S, GB, D], F32)
        y1_hi = m.sb("y1_hi", [P, KD, T], F32R)
        y1_lo = m.sb("y1_lo", [P, KD, T], F32R)
        wq_raw = m.sb("wq_raw", [P, KD, D], F32)
        wq_hi = m.sb("wq_hi", [P, KD, D], F32R)
        wq_lo = m.sb("wq_lo", [P, KD, D], F32R)
        q_out = [m.sb(f"q_out{i}", [P, 2, T], F32R) for i in range(2)]
        stats = m.sb("stats", [S, 2, 6], F32)
        mv = m.sb("mv", [S, 2], F32)
        var_eps = m.sb("var_eps", [S, 1], F32)
        rstd = m.sb("rstd", [S, 1], F32)
        neg_half = m.sb("neg_half", [S, 1], F32)
        p_tok = m.ps("p_tok", [S, D], F32)
        p_turn = [m.ps(f"p_turn{i}", [P, 4, P], F32) for i in range(2)]
        p_q = [m.ps(f"p_q{i}", [P, 512], F32) for i in range(2)]
        names = ("w_loaded", "w_hi_done", "w_split", "loaded", "tok", "added", "ready", "rooted", "normed",
                 "turned", "t_hi", "t_lo", "proj", "q_hi", "q_lo", "y1_stored", "half")
        (w_loaded, w_hi_done, w_split, loaded, tok, added, ready, rooted, normed,
         turned, t_hi, t_lo, proj, q_hi, q_lo, y1_stored, half) = (m.sem(n) for n in names)
        q_stored = [m.sem(f"q_stored{i}") for i in range(2)]
        block = ctx.enter_context(nc.Block())

        @block.sync
        def _(sp):
            for s in (y1_stored, *q_stored):
                sp.sem_inc(s, 1)
            sp.dma_start(wq_raw[:], w_q).then_inc(w_loaded, 16)
            with sp.Fori(0, G) as g:
                sp.wait_ge(added, GB * g + 1)
                sp.dma_start(y_t[0][:], y_dram[g].rearrange("k p t -> p k t")).then_inc(loaded, 16)
                sp.dma_start(xs[:], x_tok[g]).then_inc(loaded, 16)
                for b in range(GB):
                    sp.wait_ge(normed, GB * g + b + 1)
                    sp.dma_start(y1_dram[GB * g + b], y1[:, b, :]).then_inc(y1_stored, 16)
                for j in range(KV):
                    sp.wait_ge(q_lo, KV * g + j + 3)
                    for s in range(2):
                        sp.dma_start(qd[g, :, s].rearrange("b p m q -> p m b q")[:, j],
                                     q_out[j % 2][:, s, :].bitcast(F32).rearrange("p (b q) -> p b q", q=S)).then_inc(q_stored[j % 2], 16)
            sp.wait_ge(y1_stored, 16 * B + 1)
            for s in q_stored:
                sp.wait_ge(s, 16 * G * KV + 1)

        @block.gpsimd
        def _(pool):
            nc.gpsimd.memset(neg_half[:], -0.5).then_inc(half, 1)
            pool.wait_ge(w_hi_done, 1)
            nc.gpsimd.tensor_tensor(wq_lo[:], wq_raw[:], wq_hi[:].bitcast(F32), ALU.subtract).then_inc(w_split, 1)
            pool.wait_ge(half, 1)
            with pool.Fori(0, B) as n:
                pool.wait_ge(ready, n + 1)
                nc.gpsimd.tensor_tensor(rstd[:], var_eps[:], neg_half[:], ALU.pow).then_inc(rooted, 1)

        @block.scalar
        def _(act):
            act.wait_ge(w_loaded, 16)
            nc.scalar.copy(wq_hi[:], wq_raw[:]).then_inc(w_hi_done, 1)
            with act.Fori(0, G) as g:
                for b in range(GB):
                    for i in range(2):
                        act.wait_ge(turned, 2 * GB * g + 2 * b + i + 1)
                        if b == 0 and i == 0:
                            act.wait_ge(proj, KV * g + 1)
                        nc.scalar.copy(y1_hi[:, 4 * i:4 * i + 4, b * S:(b + 1) * S],
                                       p_turn[i][:, :, 0:S]).then_inc(t_hi, 1)
                for j in range(KV):
                    act.wait_ge(proj, KV * g + j + 2)
                    act.wait_ge(q_stored[j % 2], 16 * KV * g + 32 * (j // 2) + 1)
                    nc.scalar.copy(q_out[j % 2][:, 0, :], p_q[j % 2][:, 0:T]).then_inc(q_hi, 1)

        @block.vector
        def _(dve):
            dve.sem_inc(t_lo, 2)
            dve.sem_inc(q_lo, 2)
            dve.sem_inc(added, 1)
            with dve.Fori(0, G) as g:
                def lo_part(b):
                    for i in range(2):
                        dve.wait_ge(t_hi, 2 * GB * g + 2 * b + i + 1)
                        nc.vector.tensor_tensor(y1_lo[:, 4 * i:4 * i + 4, b * S:(b + 1) * S], p_turn[i][:, :, 0:S],
                                                y1_hi[:, 4 * i:4 * i + 4, b * S:(b + 1) * S].bitcast(F32),
                                                ALU.subtract).then_inc(t_lo, 1)

                dve.wait_ge(y1_stored, 16 * GB * g + 1)
                for b in range(GB):
                    dve.wait_ge(tok, GB * g + b + 1)
                    nc.vector.tensor_tensor(xs[:, b, :], xs[:, b, :], p_tok[:], ALU.add).then_inc(added, 1)
                    dve.drain()
                    layer_norm(nc, dve, xs[:, b, :], stats, mv, var_eps, rstd, y1[:, b, :], ready, rooted,
                               GB * g + b + 1).then_inc(normed, 1)
                    if b >= 1:
                        lo_part(b - 1)
                lo_part(GB - 1)
                for j in range(KV):
                    dve.wait_ge(q_hi, KV * g + j + 1)
                    nc.vector.tensor_tensor(q_out[j % 2][:, 1, :], p_q[j % 2][:, 0:T],
                                            q_out[j % 2][:, 0, :].bitcast(F32), ALU.subtract).then_inc(q_lo, 1)

        @block.tensor
        def _(pe):
            pe.sem_inc(proj, 1)
            pe.wait_ge(w_split, 1)
            with pe.Fori(0, G) as g:
                def to_tokens(b):
                    pe.wait_ge(added, GB * g + b + 1)
                    for k in range(KD):
                        last = nc.tensor.transpose(p_tok[:, k * P:(k + 1) * P], y_t[0][:, k, b * S:(b + 1) * S],
                                                   ident_f[:])
                    last.then_inc(tok, 1)

                pe.wait_ge(loaded, 32 * g + 32)
                to_tokens(0)
                for b in range(GB):
                    if b + 1 < GB:
                        to_tokens(b + 1)
                    pe.wait_ge(normed, GB * g + b + 1)
                    for i in range(2):
                        pe.wait_ge(t_lo, 2 * GB * g + 2 * b + i + 1)
                        for k in range(4):
                            kk = 4 * i + k
                            last = nc.tensor.transpose(p_turn[i][:, k, 0:S], y1[:, b, kk * P:(kk + 1) * P],
                                                       ident_f[0:S, 0:S])
                        last.then_inc(turned, 1)
                pe.wait_ge(t_lo, 2 * GB * g + 2 * GB + 2)
                for j in range(KV):
                    pe.wait_ge(q_lo, KV * g + j + 1)
                    for k in range(KD):
                        w = slice(j * P, (j + 1) * P)
                        last = matmul3(nc, p_q[j % 2][:, 0:T], wq_hi[:, k, w], wq_lo[:, k, w],
                                       y1_hi[:, k, :], y1_lo[:, k, :], k == 0, k == KD - 1)
                    last.then_inc(proj, 1)


def attention_pass(nc, kd, vd, qd, y1_dram, w_o, w3_dram, ident_f, out):
    STACK = 3 * HD
    KR = STACK + 2
    with ExitStack() as ctx:
        m = Bufs(nc, ctx, "ap")
        qs = [m.sb(f"qs{i}", [KR, REP, KV, S], F32R) for i in range(2)]
        ks = [m.sb(f"ks{i}", [KR, 2, 4, CP], F32R) for i in range(2)]
        vs = [m.sb(f"vs{i}", [KN, KT, KV, VW], F32) for i in range(2)]
        y1 = [m.sb(f"y1{i}", [S, D], F32) for i in range(2)]
        probs = [m.sb(f"probs{i}", [KN, KT, T], F32) for i in range(2)]
        wo_raw = [m.sb(f"wo_raw{i}", [P, D], F32) for i in range(2)]
        wo_hi = m.sb("wo_hi", [P, KD, D], F32R)
        wo_lo = m.sb("wo_lo", [P, KD, D], F32R)
        w3 = m.sb("w3", [P, KD, D], BF16)
        n_max = m.sb("n_max", [S, H], F32)
        nm_hi = m.sb("nm_hi", [H, S], F32R)
        nm_lo = m.sb("nm_lo", [H, S], F32R)
        o_num = [m.sb(f"o_num{i}", [P, T], F32) for i in range(2)]
        o_den = [m.sb(f"o_den{i}", [P, T], F32) for i in range(2)]
        o_t = m.sb("o_t", [P, KD, S], F32)
        o_hi = m.sb("o_hi", [P, KD, S], F32R)
        o_lo = m.sb("o_lo", [P, KD, S], F32R)
        y2 = m.sb("y2", [S, D], F32)
        y2_t = m.sb("y2_t", [P, KD, S], BF16)
        lin = m.sb("lin", [S, D], BF16)
        fin = m.sb("fin", [S, D], F32)
        stats = m.sb("stats", [S, 2, 6], F32)
        mv = m.sb("mv", [S, 2], F32)
        var_eps = m.sb("var_eps", [S, 1], F32)
        rstd = m.sb("rstd", [S, 1], F32)
        neg_half = m.sb("neg_half", [S, 1], F32)
        p_s = [m.ps(f"p_s{i}", [S, 512], F32) for i in range(2)]
        p_t = [m.ps(f"p_t{i}", [P, 512], F32) for i in range(2)]
        p_o = m.ps("p_o", [P, 512], F32)
        p_turn = m.ps("p_turn", [P, 512], F32)
        p_y = m.ps("p_y", [S, D], F32)
        names = ("w_loaded", "ones", "half", "scored", "maxed", "nm_turned", "nmh", "nml", "t_scored", "exped",
                 "pv", "o_taken", "normed_o", "o_hi_done", "turned", "turn_read", "proj", "y2_done", "lin_mm", "lin_done",
                 "ready", "rooted", "o_lo_done", "fin_done", "wo_hi_done", "wo_lo_done")
        (w_loaded, ones, half, scored, maxed, nm_turned, nmh, nml, t_scored, exped,
         pv, o_taken, normed_o, o_hi_done, turned, turn_read, proj, y2_done, lin_mm, lin_done,
         ready, rooted, o_lo_done, fin_done, wo_hi_done, wo_lo_done) = (m.sem(n) for n in names)
        loaded = [m.sem(f"loaded{i}") for i in range(2)]
        wo_loaded = [m.sem(f"wo_loaded{i}") for i in range(2)]
        nm_put = m.sem("nm_put")
        stored = m.sem("stored")
        block = ctx.enter_context(nc.Block())
        N_LOAD = 3 + 6 + 1 + 1
        AHEAD = (0, 0, 6, 6, 4, 6, 6, 4)
        BEHIND = 1
        GROUPS = ((0, 1, 2), (3, 4, 5), (6, 7))
        NG = len(GROUPS)
        GROUP_OF = {h: g for g, heads in enumerate(GROUPS) for h in heads}

        def ahead(h):
            return range(sum(AHEAD[:h]), sum(AHEAD[:h + 1]))

        def turns(eng, turn):
            turn(0, 0, True, False)
            with eng.Fori(0, B // 2 - 1) as i:
                turn(2 * i + 1, 1, True, True)
                turn(2 * i + 2, 0, True, True)
            turn(B - 1, 1, False, True)

        @block.sync
        def _(sp):
            def load(n, p):
                sp.wait_ge(pv, KV * n - KV + 2)
                fetch(n, p)

            def fetch(n, p):
                for part, s in enumerate((0, 0, 1)):
                    sp.dma_start(qs[p][part * HD:(part + 1) * HD].bitcast(F32).rearrange("d j m q -> d j (m q)"),
                                 qd[n, s]).then_inc(loaded[p], 16)
                for part, s in enumerate((0, 1, 0)):
                    for mk in range(2):
                        sp.dma_start(ks[p][part * HD:(part + 1) * HD, mk].bitcast(F32),
                                     kd[n, mk, s]).then_inc(loaded[p], 16)
                sp.dma_start(vs[p][:].rearrange("p t v w -> p (t v w)"), vd[n]).then_inc(loaded[p], 16)
                if not isinstance(n, int) or n > 1:
                    sp.wait_ge(y2_done, n)
                sp.dma_start(y1[p][:], y1_dram[n]).then_inc(loaded[p], 16)

            def put_max(n, p):
                sp.wait_ge(nml, n + 1)
                sp.dma_start(qs[p][STACK:STACK + 1].bitcast(F32).rearrange("o j m q -> o (j m) q"),
                             nm_hi[:].bitcast(F32)).then_inc(nm_put, 16)
                sp.dma_start(qs[p][STACK + 1:KR].bitcast(F32).rearrange("o j m q -> o (j m) q"),
                             nm_lo[:].bitcast(F32)).then_inc(nm_put, 16)

            def store(n):
                sp.wait_ge(fin_done, n + 1)
                sp.dma_start(out[n], fin[:]).then_inc(stored, 16)

            def turn(n, p, next_, last_):
                if next_:
                    load(n + 1, 1 - p)
                if last_:
                    store(n - 1)
                if next_:
                    put_max(n + 1, 1 - p)

            sp.sem_inc(nm_put, 1)
            sp.sem_inc(stored, 1)
            fetch(0, 0)
            sp.dma_start(w3[:], w3_dram).then_inc(w_loaded, 16)
            for k in range(KD):
                if k >= 2:
                    sp.wait_ge(wo_lo_done, k - 1)
                sp.dma_start(wo_raw[k % 2][:], w_o[:, k, :]).then_inc(wo_loaded[k % 2], 16)
            put_max(0, 0)
            turns(sp, turn)
            store(B - 1)
            sp.wait_ge(stored, 16 * B + 1)

        @block.gpsimd
        def _(pool):
            nc.gpsimd.memset(neg_half[:], -0.5).then_inc(half, 1)
            pool.wait_ge(half, 1)
            for p in range(2):
                nc.gpsimd.memset(ks[p][STACK:KR].bitcast(F32), 1.0).then_inc(ones, 1)
            pool.wait_ge(ones, 2)
            for k in range(KD):
                pool.wait_ge(wo_hi_done, k + 1)
                nc.gpsimd.tensor_tensor(wo_lo[:, k, :], wo_raw[k % 2][:], wo_hi[:, k, :].bitcast(F32),
                                        ALU.subtract).then_inc(wo_lo_done, 1)
            pool.wait_ge(wo_lo_done, KD)

            def root(x):
                pool.wait_ge(ready, x + 1)
                nc.gpsimd.tensor_tensor(rstd[:], var_eps[:], neg_half[:], ALU.pow).then_inc(rooted, 1)

            def turn(n, p, next_, last_):
                for g in range(NG):
                    if last_ and g == 0:
                        root(2 * n - 1)
                        pool.wait_ge(rooted, 2 * n)
                    heads = slice(GROUPS[g][0], GROUPS[g][-1] + 1)
                    pool.wait_ge(o_hi_done, NG * n + g + 1)
                    nc.gpsimd.tensor_tensor(o_lo[:, heads, :], o_t[:, heads, :], o_hi[:, heads, :].bitcast(F32),
                                            ALU.subtract).then_inc(o_lo_done, 1)
                pool.wait_ge(o_lo_done, NG * n + NG + NG)
                root(2 * n)
                pool.wait_ge(rooted, 2 * n + 1)

            pool.sem_inc(o_lo_done, NG)
            turns(pool, turn)
            root(2 * B - 1)

        @block.scalar
        def _(act):
            def max_hi(n):
                act.wait_ge(nm_turned, n + 1)
                if not isinstance(n, int) or n > 0:
                    act.wait_ge(nm_put, 32 * n + 1)
                nc.scalar.activation(nm_hi[:], p_turn[0:H, 0:S], ACT.Copy, scale=-1.0).then_inc(nmh, 1)

            def evacuate(dst, count):
                for i in range(2):
                    act.wait_ge(turned, count + i + 1)
                    nc.scalar.copy(dst[:, 4 * i:4 * i + 4, :],
                                   p_turn[:].rearrange("p (k s) -> p k s", k=4)[:, :, 0:S]).then_inc(turn_read, 1)

            def take(n, p, h):
                g = GROUP_OF[h]
                buf, rows = (p * NG + g) % 2, slice((h - GROUPS[g][0]) * HD, (h - GROUPS[g][0] + 1) * HD)
                act.wait_ge(pv, KV * n + h + 3)
                if h == GROUPS[g][0]:
                    act.wait_ge(normed_o, NG * n + g - 2 + 1 + NG)
                nc.scalar.copy(o_num[buf][rows, :], p_o[0:HD, 0:T])
                nc.scalar.copy(o_den[buf][rows, :], p_o[HD:2 * HD, 0:T]).then_inc(o_taken, 1)

            def split_hi(n, g):
                heads = slice(GROUPS[g][0], GROUPS[g][-1] + 1)
                act.wait_ge(normed_o, NG * n + g + 1 + NG)
                if g == 0:
                    act.wait_ge(proj, n + 1)
                nc.scalar.copy(o_hi[:, heads, :], o_t[:, heads, :]).then_inc(o_hi_done, 1)

            def behind(n):
                evacuate(y2_t, 2 * n)
                act.wait_ge(lin_mm, n + 1)
                nc.scalar.copy(lin[:], p_y[:]).then_inc(lin_done, 1)

            def turn(n, p, next_, last_):
                for h in range(KV):
                    for t in range(KT):
                        x = h * KT + t
                        act.wait_ge(t_scored, KV * KT * n + x + 1)
                        if t == 0:
                            act.wait_ge(pv, KV * n + h + 1)
                        nc.scalar.activation(probs[h % 2][:, t, :], p_t[x % 2][0:KN, 0:T], ACT.Exp,
                                             scale=SCALE).then_inc(exped, 1)
                    if h >= 1:
                        take(n, p, h - 1)
                    if last_ and h == BEHIND:
                        behind(n - 1)
                    if h >= 3 and h - 3 == GROUPS[GROUP_OF[h - 3]][-1]:
                        split_hi(n, GROUP_OF[h - 3])
                if next_:
                    max_hi(n + 1)
                split_hi(n, NG - 2)
                take(n, p, KV - 1)
                split_hi(n, NG - 1)

            act.sem_inc(turn_read, 1)
            act.sem_inc(exped, 2)
            act.sem_inc(o_taken, 1)
            act.sem_inc(lin_done, 1)
            for k in range(KD):
                act.wait_ge(wo_loaded[k % 2], 16 * (k // 2 + 1))
                nc.scalar.copy(wo_hi[:, k, :], wo_raw[k % 2][:]).then_inc(wo_hi_done, 1)
            max_hi(0)
            turns(act, turn)
            behind(B - 1)

        @block.vector
        def _(dve):
            def maxima(n, xs):
                for x in xs:
                    h, j = divmod(x, REP)
                    dve.wait_ge(scored, H * n + x + 1)
                    nc.vector.reduce_max(n_max[:, j * KV + h:j * KV + h + 1], p_s[x % 2][:, 0:C],
                                         AX_X).then_inc(maxed, 1)

            def max_lo(n):
                dve.wait_ge(nmh, n + 1)
                nc.vector.scalar_tensor_tensor(out=nm_lo[:], in0=p_turn[0:H, 0:S], scalar=-1.0,
                                               in1=nm_hi[:].bitcast(F32), op0=ALU.mult,
                                               op1=ALU.subtract).then_inc(nml, 1)

            def divide(n, p, g):
                buf, rows = (p * NG + g) % 2, len(GROUPS[g]) * HD
                dve.wait_ge(o_taken, KV * n + GROUPS[g][-1] + 2)
                dve.wait_ge(o_lo_done, NG * n + g + 1)
                for half_ in (slice(0, T // 2), slice(T // 2, T)):
                    nc.vector.reciprocal(o_den[buf][0:rows, half_], o_den[buf][0:rows, half_])
                    yield
                dve.drain()
                for r, h in enumerate(GROUPS[g]):
                    for j in range(REP):
                        q = slice(j * S, (j + 1) * S)
                        last = nc.vector.tensor_tensor(o_t[j * HD:(j + 1) * HD, h, :],
                                                       o_num[buf][r * HD:(r + 1) * HD, q],
                                                       o_den[buf][r * HD:(r + 1) * HD, q], ALU.mult)
                    if h == GROUPS[g][-1]:
                        last.then_inc(normed_o, 1)
                    yield

            def behind(n):
                dve.wait_ge(lin_done, n + 2)
                dve.wait_ge(stored, 16 * n + 1)
                nc.vector.tensor_tensor(fin[:], lin[:], y2[:], ALU.add)
                dve.drain()
                layer_norm(nc, dve, fin[:], stats, mv, var_eps, rstd, fin[:], ready, rooted,
                           2 * n + 2).then_inc(fin_done, 1)

            def turn(n, p, next_, last_):
                for h in range(KV):
                    whole_group = h >= 2 and h - 2 == GROUPS[GROUP_OF[h - 2]][-1]
                    steps = divide(n, p, GROUP_OF[h - 2]) if whole_group else iter(())
                    for x in ahead(h) if next_ else ():
                        maxima(n + 1, (x,))
                        next(steps, None)
                    for _ in steps:
                        pass
                    if last_ and h == BEHIND + 1:
                        behind(n - 1)
                if next_:
                    max_lo(n + 1)
                for _ in divide(n, p, NG - 1):
                    pass
                dve.wait_ge(proj, n + 2)
                nc.vector.tensor_tensor(y2[:], p_y[:], y1[p][:], ALU.add)
                dve.drain()
                layer_norm(nc, dve, y2[:], stats, mv, var_eps, rstd, y2[:], ready, rooted,
                           2 * n + 1).then_inc(y2_done, 1)

            dve.sem_inc(maxed, 2)
            dve.sem_inc(normed_o, NG)
            dve.sem_inc(y2_done, 1)
            maxima(0, range(H))
            max_lo(0)
            turns(dve, turn)
            behind(B - 1)

        @block.tensor
        def _(pe):
            def first_scores(n, p, xs, most):
                for _, x in zip(range(most), xs):
                    h, j = divmod(x, REP)
                    pe.wait_ge(maxed, H * n + x + 1)
                    nc.tensor.matmul(p_s[x % 2][:, 0:CP], qs[p][0:STACK, j, h, :],
                                     ks[p][0:STACK, h // 4, h % 4, :], start=True, stop=True).then_inc(scored, 1)

            def turn_maxima(n, reads):
                pe.wait_ge(maxed, H * n + H + 2)
                pe.wait_ge(turn_read, reads + 1)
                nc.tensor.transpose(p_turn[0:H, 0:S], n_max[:], ident_f[0:S, 0:S]).then_inc(nm_turned, 1)

            def second_scores(n, p, h, between):
                for t in range(KT):
                    x = h * KT + t
                    pe.wait_ge(exped, KV * KT * n + x + 1)
                    nc.tensor.matmul(p_t[x % 2][0:KN, 0:T], ks[p][0:KR, h // 4, h % 4, t * KN:(t + 1) * KN],
                                     qs[p][:, :, h, :], start=True, stop=True).then_inc(t_scored, 1)
                    between()

            def values(n, p, h, between):
                pe.wait_ge(exped, KV * KT * n + KT * h + KT + 2)
                pe.wait_ge(o_taken, KV * n + h + 1)
                for t in range(KT):
                    last = nc.tensor.matmul(p_o[0:VW, 0:T], vs[p][:, t, h, :], probs[h % 2][:, t, :],
                                            start=(t == 0), stop=(t == KT - 1))
                    if t == KT - 1:
                        last.then_inc(pv, 1)
                    between()

            def turn_both(src, count):
                for i in range(2):
                    pe.wait_ge(turn_read, count + i + 1)
                    for k in range(4):
                        kk = 4 * i + k
                        last = nc.tensor.transpose(p_turn[:, k * P:k * P + S], src[:, kk * P:(kk + 1) * P],
                                                   ident_f[0:S, 0:S])
                    last.then_inc(turned, 1)
                pe.wait_ge(turn_read, count + 3)

            def linear():
                for c in range(2):
                    cols = slice(c * 512, (c + 1) * 512)
                    for k in range(KD):
                        last = nc.tensor.matmul(p_y[:, cols], y2_t[:, k, :], w3[:, k, cols],
                                                start=(k == 0), stop=(k == KD - 1))
                last.then_inc(lin_mm, 1)

            def behind(n):
                pe.wait_ge(y2_done, n + 2)
                pe.wait_ge(nml, n + 2 if not isinstance(n, int) or n < B - 1 else B)
                turn_both(y2, 2 * n)
                linear()

            def turn(n, p, next_, last_):
                pe.wait_ge(nm_put, 32 * n + 33)
                for h in range(KV):
                    xs = iter(ahead(h) if next_ else ())
                    if next_ and sum(AHEAD[:h]) == 0 < AHEAD[h]:
                        await_load(n + 1, 1 - p)

                    def between():
                        first_scores(n + 1, 1 - p, xs, 1)

                    second_scores(n, p, h, between)
                    if h >= 1:
                        values(n, p, h - 1, between)
                    if last_ and h == BEHIND:
                        behind(n - 1)
                if next_:
                    turn_maxima(n + 1, 2 * n)
                values(n, p, KV - 1, lambda: None)
                pe.wait_ge(lin_done, n + 1)
                for g, heads in enumerate(GROUPS):
                    pe.wait_ge(o_lo_done, NG * n + g + 1 + NG)
                    for c in range(2):
                        cols = slice(c * 512, (c + 1) * 512)
                        for k in heads:
                            last = matmul3(nc, p_y[:, cols], o_hi[:, k, :], o_lo[:, k, :], wo_hi[:, k, cols],
                                           wo_lo[:, k, cols], k == 0, k == KD - 1)
                last.then_inc(proj, 1)

            def await_load(n, p):
                if isinstance(n, int):
                    pe.wait_ge(loaded[p], 16 * N_LOAD * (n // 2 + 1))
                else:
                    pe.wait_ge(loaded[p], 8 * N_LOAD * (n + 2 - p))

            pe.sem_inc(pv, 2)
            pe.sem_inc(proj, 1)
            pe.wait_ge(ones, 2)
            await_load(0, 0)
            first_scores(0, 0, iter(range(H)), H)
            turn_maxima(0, 0)
            pe.wait_ge(w_loaded, 16)
            pe.wait_ge(wo_lo_done, KD)
            turns(pe, turn)
            behind(B - 1)


def make_identities(nc, ident_f, ident_b):
    with ExitStack() as ctx:
        zeroed = ctx.enter_context(nc.semaphore("id_zeroed"))
        made = ctx.enter_context(nc.semaphore("id_made"))
        block = ctx.enter_context(nc.Block())

        @block.gpsimd
        def _(pool):
            nc.gpsimd.memset(ident_f[:], 0.0).then_inc(zeroed, 1)
            pool.wait_ge(zeroed, 1)
            nc.gpsimd.affine_select(out=ident_f[:], in_=ident_f[:], compare_op=ALU.not_equal, fill=1.0, base=0,
                                    pattern=[[-1, P]], channel_multiplier=1).then_inc(made, 1)
            pool.wait_ge(made, 1)
            nc.gpsimd.tensor_copy(ident_b[:], ident_f[:]).then_inc(made, 1)


def build(nc, a, out):
    kd = nc.dram_tensor("k_scratch", (B, P, 2 * 2 * CP), F32, kind="Internal").ap()
    vd = nc.dram_tensor("v_scratch", (B, KN, KT * KV * VW), F32, kind="Internal").ap()
    qd = nc.dram_tensor("q_scratch", (G, GB, 2, P, KV, S), F32, kind="Internal").ap()
    yd = nc.dram_tensor("y_scratch", (G, KD, P, T), F32, kind="Internal").ap()
    y1d = nc.dram_tensor("y1_scratch", (B, S, D), F32, kind="Internal").ap()
    w3d = nc.dram_tensor("w3_scratch", (P, KD, D), BF16, kind="Internal").ap()
    with ExitStack() as ctx:
        ident_f = ctx.enter_context(nc.sbuf_tensor("ident_f", [P, P], F32))
        ident_b = ctx.enter_context(nc.sbuf_tensor("ident_b", [P, P], BF16))
        make_identities(nc, ident_f, ident_b)
        dequant_pass(nc, a["q_weight"], a["q_scale"], a["q_zero"], ident_b, w3d)
        context_pass(nc, a["ctx_t"], a["w_kv"], kd, vd)
        gated_pass(nc, a["x_t"], a["w_gu"], a["w_d"], a["w_d_tail"], ident_f, ident_b, yd)
        query_pass(nc, a["x_tok"], yd, a["w_q"], ident_f, y1d, qd)
        k_v = kd.rearrange("b (v d) (m s c) -> b m s d v c", d=HD, m=2, s=2)
        q_v = qd.rearrange("g b s (j d) m q -> (g b) s d j (m q)", d=HD)
        attention_pass(nc, k_v, vd, q_v, y1d, a["w_o"], w3d, ident_f, out)


def kernel(x, ctx_4096, L0_attn_w_gate, L0_attn_w_up, L0_attn_w_down, L0_xattn_Wq, L0_xattn_Wk, L0_xattn_Wv,
           L0_xattn_Wo, L0_ffn_qweight, L0_ffn_qscale, L0_ffn_qzeros):
    import numpy as np
    import concourse.bacc as bacc
    from concourse.bass_utils import run_bass_kernel_spmd as run

    def tiles(w):
        w = np.asarray(w)
        return np.ascontiguousarray(w.reshape(-1, P, w.shape[1]).transpose(1, 0, 2))

    x = np.asarray(x)
    ctx_ = np.asarray(ctx_4096)
    wd = np.asarray(L0_attn_w_down)
    wd_full = wd[:, :MI_FULL * P].reshape(KD, P, MI_FULL, P)
    wd_tail = wd[:, MI_FULL * P:].reshape(KD, P, TAIL)
    arrays = {
        "x_t": np.ascontiguousarray(x.reshape(G, T, KD, P).transpose(0, 3, 2, 1)),
        "x_tok": np.ascontiguousarray(x.reshape(G, GB, S, D).transpose(0, 2, 1, 3)),
        "ctx_t": np.ascontiguousarray(ctx_.reshape(B, C, KD, P).transpose(0, 3, 2, 1)),
        "w_gu": np.stack([tiles(np.asarray(L0_attn_w_gate).T), tiles(np.asarray(L0_attn_w_up).T)]),
        "w_d": np.ascontiguousarray(wd_full.transpose(0, 3, 2, 1)),
        "w_d_tail": np.ascontiguousarray(wd_tail.transpose(0, 2, 1)),
        "w_kv": tiles(np.concatenate([np.asarray(L0_xattn_Wk), np.asarray(L0_xattn_Wv)], axis=1)),
        "w_q": tiles(L0_xattn_Wq),
        "w_o": tiles(L0_xattn_Wo),
        "q_weight": np.asarray(L0_ffn_qweight),
        "q_scale": np.ascontiguousarray(np.asarray(L0_ffn_qscale).reshape(NQ, KD, P).transpose(2, 1, 0)),
        "q_zero": np.ascontiguousarray(np.asarray(L0_ffn_qzeros).reshape(NQ, KD, P).transpose(2, 1, 0)),
    }
    nc = bacc.Bacc("TRN2", target_bir_lowering=False, num_devices=1)
    aps = {n: nc.dram_tensor(f"in_{n}", v.shape, mybir.dt.from_np(v.dtype), kind="ExternalInput").ap()
           for n, v in arrays.items()}
    out = nc.dram_tensor("out_0", (B, S, D), F32, kind="ExternalOutput").ap()
    build(nc, aps, out)
    r = run(nc, [{f"in_{n}": v for n, v in arrays.items()}], core_ids=[0])
    return r.results[0]["out_0"]
```
